# Optimizing a Trainium2 kernel written in Bass

```python
import numpy as np
import jax
import jax.numpy as jnp

def _softmax(x, axis=-1):
    return jax.nn.softmax(x, axis=axis)
def _gelu(x):
    return jax.nn.gelu(x, approximate=True)
def _silu(x):
    return jax.nn.silu(x)
def _sigmoid(x):
    return jax.nn.sigmoid(x)
def _layernorm(x, axis=-1, eps=1e-5):
    m = jnp.mean(x, axis=axis, keepdims=True)
    v = jnp.var(x, axis=axis, keepdims=True)
    return (x - m) / jnp.sqrt(v + eps)
def _scatter_add(tgt, idx, src, axis=0):
    return tgt.at[idx].add(src)
def _segment_sum(src, seg, n):
    return jax.ops.segment_sum(src, seg, n)

kernel_name = 'mk_adj_preln_d1_adj_256_5315cd'

def setup_inputs(seed: int = 0):
    np.random.seed(seed)
    _w = jnp.asarray
    def _rec_inputs():
        import jax
        import jax.numpy as jnp
        _gk = jax.random.key(seed)
        x = -0.0005207 + 1.001 * jax.random.normal(jax.random.fold_in(_gk, 1), (8192, 256), jnp.float32)
        _a = jax.random.bernoulli(jax.random.fold_in(_gk, 2), 0.00390625, (8192, 8192))
        adj = _a.astype(jnp.int32)
        return x, adj
    x, adj = _rec_inputs()
    def _L0_gnn_setup():
        import jax, jax.numpy as jnp
        import numpy as np
        N, F_IN, F_OUT = (8192, 256, 256)
        ALPHA = 0.2
        NEG = -9000000000000000.0
        key = jax.random.key(seed)
        k1, k2, k3, k4, k5 = jax.random.split(key, 5)
        h = jax.random.normal(k1, (N, F_IN), dtype=jnp.float32)
        adj = jax.random.randint(k2, (N, N), 0, 2, dtype=jnp.int32)
        W_w = jax.random.normal(k3, (F_IN, F_OUT), dtype=jnp.float32) / np.sqrt(F_IN)
        W_b = jax.random.normal(k4, (F_OUT,), dtype=jnp.float32) * 0.01
        a = jax.random.normal(k5, (2 * F_OUT, 1), dtype=jnp.float32) / np.sqrt(2 * F_OUT)
        return {'h': h, 'adj': adj, 'W_w': W_w, 'W_b': W_b, 'a': a}
    _L0_gnn_all = _L0_gnn_setup()
    _L0_gnn_in = {k: v for k, v in _L0_gnn_all.items() if k in ('W_w', 'W_b', 'a', )}
    del _L0_gnn_all

    return {
        "x": x,
        "adj": adj,
        "L0_gnn_W_w": _L0_gnn_in["W_w"],
        "L0_gnn_W_b": _L0_gnn_in["W_b"],
        "L0_gnn_a": _L0_gnn_in["a"],
    }

def reference(x, adj, L0_gnn_W_w, L0_gnn_W_b, L0_gnn_a):
    import jax
    import jax.numpy as jnp
    def _L0_gnn_ref(h, adj, W_w, W_b, a):
        import jax, jax.numpy as jnp
        import numpy as np
        N, F_IN, F_OUT = (8192, 256, 256)
        ALPHA = 0.2
        NEG = -9000000000000000.0
        Wh = h @ W_w + W_b
        a1 = a[:F_OUT, 0]
        a2 = a[F_OUT:, 0]
        e = jax.nn.leaky_relu((Wh @ a1)[:, None] + (Wh @ a2)[None, :], negative_slope=ALPHA)
        attention = jnp.where(adj > 0, e, NEG)
        attention = jax.nn.softmax(attention, axis=1)
        h_prime = attention @ Wh
        return h_prime

    h = jnp.maximum(_layernorm(x, axis=-1), 0.0)
    x = x + _L0_gnn_ref(h, adj, L0_gnn_W_w, L0_gnn_W_b, L0_gnn_a)
    return x


_drawn_inputs = setup_inputs


def setup_inputs(seed=0):
    import zlib

    import numpy as np

    out = dict(_drawn_inputs(seed))
    spreads = {}
    factors = {'L0_gnn_W_b': 6.633}
    for name, (base, spread) in spreads.items():
        noise = np.random.default_rng([zlib.crc32(name.encode()), seed]).standard_normal(out[name].shape)
        drawn = base * np.exp(spread * noise) if base else spread * noise
        out[name] = jnp.asarray(drawn.astype(out[name].dtype))
    for name, factor in factors.items():
        out[name] = (out[name] * factor).astype(out[name].dtype)
    return out
```

```python
import concourse.bass as bass
from concourse import mybir
from contextlib import ExitStack

F32 = mybir.dt.float32
F16 = mybir.dt.float16
BF16 = mybir.dt.bfloat16
I32 = mybir.dt.int32
ALU = mybir.AluOpType
ACT = mybir.ActivationFunctionType
AX = mybir.AxisListType
RMAX = bass.bass_isa.ReduceOp.max
RADD = bass.bass_isa.ReduceOp.add

P = 128
QP = 32
NQ = P // QP
SLOPE = 0.2
EPS = 1e-5
EXPONENT = 0x7F800000
HEADROOM = 2.0 ** 11


def gat_layer(nc, x, adj, W_w, W_b, a, out):
    N, F = x.shape
    F1 = F + 1
    F2 = F + 2
    SLOT = F2
    JQ = N // NQ
    NB = JQ // QP
    G = 8
    NG = NB // G
    R = 2 * P
    NSB = N // R
    NR = N // P
    SQ = NSB // NQ
    KF = F // P
    XG = 16

    x_cols = x.rearrange("(a b c) f -> a c b f", a=NQ, b=NB)
    x_rows = x.rearrange("(s e m) f -> s m e f", e=2, m=P)
    out_rows = out.rearrange("(s e m) f -> s m e f", e=2, m=P)
    adj_v = adj.rearrange("(s q r) (a g j) -> s a g r q j", q=R // QP, r=QP, a=NQ, g=NG)
    srow = nc.dram_tensor("neg_s_rows", [NQ, SQ * R], F32)
    srow_by_block = srow.ap().rearrange("a (w i) -> (a w) i", w=SQ)

    ctx = ExitStack()
    with ctx:
        def sb(name, shape, dt):
            return ctx.enter_context(nc.sbuf_tensor(name, shape, dt))

        def sem(name):
            return ctx.enter_context(nc.semaphore(name))

        X = sb("X", [P, NB, 4 * SLOT], F16)
        Xp = X[:, :, :].rearrange("p b (k f) -> p b k f", k=4)
        Xw = X[:, :, :].bitcast(F32)
        x_in = Xw[:, :, 0:F]
        wh_s_t = Xw[:, :, F2:2 * F2]
        wh = Xw[:, :, F2:F2 + F]
        wh_one = Xw[:, :, F2:F2 + F1]
        s_in = Xw[:, :, F2 + F]
        t_in = Xw[:, :, F2 + F1]

        nat = sb("adj_rows", [P, 2, R // QP, G * QP], I32)
        rows16 = sb("adj_rows16", [P, 2, 4, G * QP, 2], BF16)
        cols16 = sb("adj_cols16", [P, G, R], BF16)
        masks = sb("masks", [P, 4, 2, G, R], BF16)
        neg_s = sb("neg_s", [P, R], F32)
        neg_s_stage = sb("neg_s_stage", [P, R], F32)
        part = sb("part", [P, 2, 2, F1], F32)
        xres = sb("xres", [P, 2, F], F32)
        res = sb("res", [P, 2, F], F32)
        den = sb("den", [P, 4, 2], F32)

        Wx = sb("Wx", [P, KF, F2], F32)
        bias = sb("bias", [P, F2], F32)
        ident = sb("ident", [P, P], F32)
        quad = sb("quad", [P, NQ], F32)
        sum_wh = sb("sum_wh", [P, F], F32)
        t_c = sb("t_c", [P, NB], F32)
        t_j = sb("t_j", [P, NB], F32)
        neg_sj = sb("neg_sj", [P, NB], F32)
        p_j = sb("p_j", [P, NB], F32)
        two_over_p = sb("two_over_p", [P, NB], F32)
        c_j = sb("c_j", [P, 2, NB], F32)
        uv = sb("uv", [P, 2, NR], F32)
        s_i = sb("s_i", [P, NR], F32)
        ext = sb("ext", [P, 2], F32)
        top = sb("top", [P, 2], F32)
        sc = sb("sc", [P, 12], F32)

        free = masks[:, :, :, :, :].rearrange("p n k b r -> p (n k b r)").bitcast(F32)

        def carve(at, *shape):
            size = 1
            for d in shape:
                size *= d
            v = free[:, at:at + size]
            if len(shape) == 2:
                v = v.rearrange("p (a b) -> p a b", a=shape[0])
            if len(shape) == 3:
                v = v.rearrange("p (a b c) -> p a b c", a=shape[0], b=shape[1])
            return v, at + size

        w_max = 4 * 2 * G * R // 2
        a_row, at = carve(0, 2, F)
        prod, at = carve(at, F)
        h, at = carve(at, 2, F)
        hT, at = carve(at, 2, F)
        st, at = carve(at, NB, 6)
        guard, at = carve(at, 2, NR)
        mv, at = carve(at, NB, 2)
        rstd, at = carve(at, NB)
        shift, at = carve(at, NB)
        wh_sum, at = carve(at, 2, F)
        ones, at = carve(at, P)
        srow_sb, at = carve(at, SQ * R)
        diag, at = carve(at, SQ * R)
        assert at <= w_max
        xt = (part[:, :, :, :].rearrange("p e k f -> p (e k f)")[:, 0:2 * F2].bitcast(F16)
              .rearrange("p (n k f) -> p n k f", n=2, k=2))

        acc = [[ctx.enter_context(nc.psum_tensor(f"acc{e}{k}", [P, 512], F32)) for k in range(2)]
               for e in range(2)]
        ps = [ctx.enter_context(nc.psum_tensor(f"ps{i}", [P, 512], F32)) for i in range(4)]
        ps_hT, ps_wh = ps[0:2], ps[2:4]

        s_par = sem("params_loaded")
        s_x = [sem(f"x_loaded{k}") for k in range(NB // XG)]
        s_nat = [sem(f"adj_loaded{k}") for k in range(2)]
        s_srow = sem("neg_s_rows_stored")
        s_stage = sem("neg_s_staged")
        s_xres = sem("xres_loaded")
        s_out = sem("out_stored")
        s_ident = sem("ident_step")
        s_wsq = sem("w_squares_in_partition")
        s_wsq_all = sem("w_squares_summed")
        s_wnorm = sem("w_norm_ready")
        s_var = sem("variance_ready")
        s_std = sem("std_ready")
        s_norm = sem("norm_factors_ready")
        s_diag = sem("diag_ready")
        s_srow_ps = sem("neg_s_rows_in_psum")
        s_scol_ps = sem("neg_s_columns_in_psum")
        s_wsum_ps = sem("sum_wh_in_psum")
        s_srow_sb = sem("neg_s_rows_ready")
        s_si = sem("s_i_ready")
        s_wsum = sem("sum_wh_ready")
        s_ext = sem("extremes_ready")
        s_top = sem("extremes_of_all_ready")
        s_dt = sem("t_centred")
        s_exp = sem("column_exps_ready")
        s_uvx = sem("row_exponents_ready")
        s_uv = sem("row_factors_ready")
        s_c = sem("column_factors_ready")
        s_chain = sem("vector_chain")
        s_bn = sem("bn_step")
        s_h = sem("h_ready")
        s_ht = sem("h_transposed")
        s_hT = sem("hT_ready")
        s_whp = sem("wh_in_psum")
        s_wh = sem("wh_ready")
        s_sum = sem("wh_summed")
        s_hi = sem("x_hi_ready")
        s_lo = sem("x_lo_ready")
        s_X = sem("X_ready")
        s_cast = sem("adj_cast")
        s_tr = sem("adj_transposed")
        s_pos = sem("gated")
        s_m1 = sem("steep_ready")
        s_m = sem("masks_ready")
        s_ns = sem("neg_s_ready")
        s_mul = sem("half_unit_multiplied")
        s_ev = [sem(f"acc{e}_evacuated") for e in range(2)]
        s_epi = sem("epilogue_step")
        s_res = sem("res_ready")

        EPI = 7

        block = ctx.enter_context(nc.Block())

        @block.sync
        def _(sp):
            for k in range(KF):
                sp.dma_start(Wx[:, k, 0:F], W_w[k * P:(k + 1) * P, :]).then_inc(s_par, 16)
            sp.dma_start(bias[:, 0:F], W_b.rearrange("(o f) -> o f", o=1).broadcast_to([P, F])).then_inc(s_par, 16)
            for k in range(2):
                sp.dma_start(a_row[:, k, :], a[k * F:(k + 1) * F, :].rearrange("f o -> o f").broadcast_to([P, F])).then_inc(s_par, 16)
            for k in range(NB // XG):
                for q in range(NQ):
                    sp.dma_start(x_in[QP * q:QP * (q + 1), k * XG:(k + 1) * XG, :],
                                 x_cols[q, :, k * XG:(k + 1) * XG, :]).then_inc(s_x[k], 16)

            def load_adj(sblk, g):
                for q in range(NQ):
                    sp.dma_start(nat[QP * q:QP * (q + 1), g % 2, :, :], adj_v[sblk, q, g]).then_inc(s_nat[g % 2], 16)

            def stage_neg_s(sblk):
                sp.dma_start(neg_s_stage[:, :], srow_by_block[bass.ds(sblk, 1), :].broadcast_to([P, R])).then_inc(s_stage, 16)

            def load_xres(sblk):
                sp.dma_start(xres[:, :, :], x_rows[sblk]).then_inc(s_xres, 16)

            def store(sblk):
                sp.dma_start(out_rows[sblk], res[:, :, :]).then_inc(s_out, 16)

            for g in range(NG):
                if g >= 2:
                    sp.wait_ge(s_cast, 2 * (g - 1))
                load_adj(0, g)
                if g == 1:
                    sp.wait_ge(s_srow_sb, 1)
                    sp.dma_start(srow.ap(), srow_sb[0:NQ, :]).then_inc(s_srow, 16)
                    sp.wait_ge(s_srow, 16)
                    stage_neg_s(0)
                if g == 6:
                    load_xres(0)
            with sp.Fori(1, NSB) as s:
                for g in range(NG):
                    sp.wait_ge(s_cast, 2 * NG * s + 2 * (g - 1))
                    load_adj(s, g)
                    if g == 0:
                        sp.wait_ge(s_ns, s)
                        stage_neg_s(s)
                    if g == 5:
                        sp.wait_ge(s_res, s)
                        store(s - 1)
                sp.wait_ge(s_out, 16 * s)
                load_xres(s)
            sp.wait_ge(s_res, NSB)
            store(NSB - 1)
            sp.wait_ge(s_out, 16 * NSB)

        @block.gpsimd
        def _(pool):
            nc.gpsimd.memset(ident[:, :], 0.0).then_inc(s_ident, 1)
            pool.wait_ge(s_ident, 1)
            nc.gpsimd.affine_select(out=ident[:, :], in_=ident[:, :], compare_op=ALU.not_equal, fill=1.0, base=0,
                                    pattern=[[-1, P]], channel_multiplier=1).then_inc(s_ident, 1)
            pool.wait_ge(s_wsq, 1)
            nc.gpsimd.partition_all_reduce(sc[:, 1:2], sc[:, 0:1], P, RADD).then_inc(s_wsq_all, 1)

            def add_wh(b, k, first):
                pool.wait_ge(s_wh, b + 1)
                if first:
                    nc.gpsimd.tensor_copy(wh_sum[:, k, :], wh[:, b, :]).then_inc(s_sum, 1)
                else:
                    pool.wait_ge(s_sum, b - 1)
                    nc.gpsimd.tensor_tensor(wh_sum[:, k, :], wh_sum[:, k, :], wh[:, b, :], ALU.add).then_inc(s_sum, 1)
            for k in range(2):
                add_wh(k, k, True)
            with pool.Fori(1, NB // 2) as pair:
                for k in range(2):
                    add_wh(2 * pair + k, k, False)
            pool.wait_ge(s_ext, 1)
            nc.gpsimd.partition_all_reduce(top[:, :], ext[:, :], P, RMAX).then_inc(s_top, 1)

            for b in range(NB):
                pool.wait_ge(s_lo, 2 * b + 2)
                nc.gpsimd.tensor_copy(Xp[:, b, 2:4, 0:F1], xt[:, b % 2, :, 0:F1]).then_inc(s_X, 1)

        @block.scalar
        def _(act):
            act.wait_ge(s_par, 16 * (KF + 3))
            nc.scalar.activation(xres[:, :, :], Wx[:, :, 0:F], ACT.Square, accum_out=sc[:, 0:1]).then_inc(s_wsq, 1)
            act.wait_ge(s_wsq_all, 1)
            nc.scalar.activation(sc[:, 2:3], sc[:, 1:2], ACT.Sqrt, scale=float(F)).then_inc(s_wnorm, 1)
            act.wait_ge(s_var, 1)
            nc.scalar.activation(rstd[:, :], rstd[:, :], ACT.Sqrt).then_inc(s_std, 1)
            act.wait_ge(s_norm, 1)

            def normalise(b, k, first):
                if not first:
                    act.wait_ge(s_ht, b - 1)
                nc.scalar.activation(h[:, k, :], x_in[:, b, :], ACT.Relu, scale=rstd[:, bass.ds(b, 1)],
                                     bias=shift[:, bass.ds(b, 1)]).then_inc(s_h, 1)

            def copy_hT(b, k, first):
                act.wait_ge(s_ht, b + 1)
                if not first:
                    act.wait_ge(s_whp, b - 1)
                nc.scalar.copy(hT[:, k, :], ps_hT[k][:, 0:F]).then_inc(s_hT, 1)

            normalise(0, 0, True)
            normalise(1, 1, True)
            copy_hT(0, 0, True)
            normalise(2, 0, False)
            copy_hT(1, 1, True)
            with act.Fori(1, NB // 2 - 1) as pair:
                for k in range(2):
                    normalise(2 * pair + k + 1, (k + 1) % 2, False)
                    copy_hT(2 * pair + k, k, False)
            normalise(NB - 1, 1, False)
            copy_hT(NB - 2, 0, False)
            copy_hT(NB - 1, 1, False)

            def cast(n, g, first):
                act.wait_ge(s_nat[g % 2], NQ * 8 * n + NQ * 8 * (2 - g % 2))
                if not first:
                    act.wait_ge(s_tr, n - 1)
                for e in range(2):
                    nc.scalar.copy(rows16[:, g % 2, :, :, e], nat[:, g % 2, 4 * e:4 * e + 4, :]).then_inc(s_cast, 1)

            act.wait_ge(s_srow_ps, 1)
            for k in range(4):
                ins = nc.scalar.copy(srow_sb[0:NQ, 512 * k:512 * (k + 1)], ps[k][0:NQ, :])
            ins.then_inc(s_srow_sb, 1)
            act.wait_ge(s_scol_ps, 1)
            s_cols = acc[0][0][:, 0:NR].rearrange("p (w e a) -> p a w e", e=2, a=NQ)
            for q in range(NQ):
                ins = nc.scalar.mul(s_i[:, q * 2 * SQ:(q + 1) * 2 * SQ].rearrange("p (w e) -> p w e", e=2),
                                    s_cols[:, q, :, :], -1.0)
            ins.then_inc(s_si, 1)
            act.wait_ge(s_wsum_ps, 1)
            nc.scalar.copy(sum_wh[:, :], acc[0][1][:, 0:F]).then_inc(s_wsum, 1)
            act.wait_ge(s_dt, 1)
            nc.scalar.activation(c_j[:, 0, :], t_c[:, :], ACT.Exp)
            nc.scalar.activation(c_j[:, 1, :], t_c[:, :], ACT.Exp, scale=SLOPE)
            nc.scalar.activation(p_j[:, :], t_c[:, :], ACT.Exp, scale=0.5 * (1.0 + SLOPE))
            nc.scalar.activation(sc[:, 6:7], sc[:, 5:6], ACT.Exp, scale=0.25 * (1.0 - SLOPE)).then_inc(s_exp, 1)
            act.wait_ge(s_uvx, 1)
            nc.scalar.activation(uv[:, :, :], uv[:, :, :], ACT.Exp).then_inc(s_uv, 1)
            for g in range(2):
                cast(g, g, True)
            act.wait_ge(s_c, 1)

            def high_parts(b, k, first):
                nc.scalar.mul(Xp[:, b, 0, 0:F1], wh_one[:, b, :], c_j[:, 0, bass.ds(b, 1)]).then_inc(s_hi, 1)
                if not first:
                    act.wait_ge(s_X, b - 1)
                nc.scalar.mul(xt[:, k, 0, 0:F1], wh_one[:, b, :], c_j[:, 1, bass.ds(b, 1)]).then_inc(s_hi, 1)

            def evacuate(sblk):
                for e in range(2):
                    act.wait_ge(s_mul, 2 * NG * sblk + 2 * NG - 1 + e)
                    for k in range(2):
                        nc.scalar.mul(part[:, e, k, :], acc[e][k][:, 0:F1],
                                      uv[:, k, bass.ds(2 * sblk + e, 1)]).then_inc(s_ev[e], 1)

            for g in range(NG):
                if g == 0:
                    high_parts(0, 0, True)
                    high_parts(1, 1, True)
                with act.Fori(g * G // 2 if g else 1, (g + 1) * G // 2) as pair:
                    for k in range(2):
                        high_parts(2 * pair + k, k, False)
                if g + 2 < NG:
                    cast(g + 2, g + 2, False)
            with act.Fori(1, NSB) as s:
                for g in range(NG):
                    cast(NG * s + g, g, False)
                    if g == 1:
                        evacuate(s - 1)
            evacuate(NSB - 1)

        @block.vector
        def _(dve):
            steps = [0]

            def step(ins):
                steps[0] += 1
                ins.then_inc(s_chain, 1)
                dve.wait_ge(s_chain, steps[0])

            dve.wait_ge(s_par, 16 * (KF + 3))
            for k in range(KF):
                for n in range(2):
                    step(nc.vector.tensor_tensor_reduce(out=prod[:, :], in0=Wx[:, k, 0:F], in1=a_row[:, n, :],
                                                        scale=1.0, scalar=0.0, op0=ALU.mult, op1=ALU.add,
                                                        accum_out=Wx[:, k, F + n:F + n + 1]))
            for n in range(2):
                step(nc.vector.tensor_tensor_reduce(out=prod[:, :], in0=bias[:, 0:F], in1=a_row[:, n, :],
                                                    scale=1.0, scalar=0.0, op0=ALU.mult, op1=ALU.add,
                                                    accum_out=bias[:, F + n:F + n + 1]))
            step(nc.vector.memset(ones[:, :], 1.0))
            step(nc.vector.tensor_reduce(sc[:, 3:4], bias[:, 0:F], AX.X, ALU.max, apply_absolute_value=True))
            step(nc.vector.memset(quad[:, :], 0.0))
            for q in range(NQ):
                step(nc.vector.memset(quad[QP * q:QP * (q + 1), q:q + 1], 1.0))
            for k in range(NB // XG):
                dve.wait_ge(s_x[k], 16 * NQ)
                for n in range(XG):
                    nc.vector.bn_stats(st[:, k * XG + n, :], x_in[:, k * XG + n, :]).then_inc(s_bn, 1)
                dve.wait_ge(s_bn, (k + 1) * XG)
                for n in range(XG):
                    ins = nc.vector.bn_aggr(mv[:, k * XG + n, :], st[:, k * XG + n, :])
            step(ins)
            nc.vector.tensor_scalar(rstd[:, :], mv[:, :, 1], EPS, None, ALU.add).then_inc(s_var, 1)
            dve.wait_ge(s_std, 1)
            step(nc.vector.reciprocal(rstd[:, :], rstd[:, :]))
            nc.vector.scalar_tensor_tensor(out=shift[:, :], in0=mv[:, :, 0], scalar=-1.0, in1=rstd[:, :],
                                           op0=ALU.mult, op1=ALU.mult).then_inc(s_norm, 1)

            def add_bias(b, k):
                dve.wait_ge(s_whp, b + 1)
                nc.vector.tensor_tensor(wh_s_t[:, b, :], ps_wh[k][:, 0:F2], bias[:, :], ALU.add).then_inc(s_wh, 1)
            with dve.Fori(0, NB // 2) as pair:
                for k in range(2):
                    add_bias(2 * pair + k, k)
            dve.wait_ge(s_wh, NB)

            step(nc.vector.tensor_scalar(neg_sj[:, :], s_in, -1.0, None, ALU.mult))
            step(nc.vector.tensor_copy(t_j[:, :], t_in))
            dve.wait_ge(s_ident, 2)
            for q in range(NQ):
                step(nc.vector.tensor_copy(prod[QP * q:QP * (q + 1), 0:QP],
                                           ident[QP * q:QP * (q + 1), QP * q:QP * (q + 1)]))
            dg = diag.rearrange("p (w q r e) -> p w q r e", w=SQ, q=4, e=2)
            ns = neg_sj[:, :].rearrange("p (w e q) -> p w q e", w=SQ, e=2)
            for w in range(SQ):
                ins = nc.vector.tensor_tensor(dg[:, w], prod[:, 0:QP].unsqueeze(1).unsqueeze(3).broadcast_to([P, 4, QP, 2]),
                                              ns[:, w].unsqueeze(2).broadcast_to([P, 4, QP, 2]), ALU.mult)
            ins.then_inc(s_diag, 1)
            nc.vector.tensor_reduce(ext[:, 0:1], t_j[:, :], AX.X, ALU.max)
            step(nc.vector.tensor_reduce(sc[:, 4:5], t_j[:, :], AX.X, ALU.min))
            nc.vector.tensor_scalar(ext[:, 1:2], sc[:, 4:5], -1.0, None, ALU.mult).then_inc(s_ext, 1)
            step(nc.vector.memset(s_in, 1.0))
            dve.wait_ge(s_wnorm, 1)
            step(nc.vector.tensor_scalar(sc[:, 3:4], sc[:, 3:4], sc[:, 2:3], 1.0, ALU.add, ALU.max))
            dve.wait_ge(s_top, 1)
            step(nc.vector.tensor_scalar(sc[:, 9:10], top[:, 0:1], top[:, 1:2], 0.5, ALU.subtract, ALU.mult))
            step(nc.vector.tensor_scalar(sc[:, 5:6], top[:, 0:1], top[:, 1:2], None, ALU.add))
            nc.vector.tensor_scalar(t_c[:, :], t_j[:, :], sc[:, 9:10], None, ALU.subtract).then_inc(s_dt, 1)
            dve.wait_ge(s_si, 1)
            step(nc.vector.tensor_scalar(guard[:, 0, :], s_i[:, :], top[:, 0:1], None, ALU.add))
            step(nc.vector.scalar_tensor_tensor(out=guard[:, 1, :], in0=guard[:, 0, :], scalar=SLOPE, in1=guard[:, 0, :],
                                                op0=ALU.mult, op1=ALU.max))
            step(nc.vector.tensor_scalar(s_i[:, :], s_i[:, :], sc[:, 9:10], None, ALU.add))
            step(nc.vector.scalar_tensor_tensor(out=uv[:, 0, :], in0=s_i[:, :], scalar=1.0, in1=guard[:, 1, :],
                                                op0=ALU.mult, op1=ALU.subtract))
            nc.vector.scalar_tensor_tensor(out=uv[:, 1, :], in0=s_i[:, :], scalar=SLOPE, in1=guard[:, 1, :],
                                           op0=ALU.mult, op1=ALU.subtract).then_inc(s_uvx, 1)
            dve.wait_ge(s_exp, 1)
            step(nc.vector.tensor_scalar(p_j[:, :].bitcast(I32), p_j[:, :].bitcast(I32), EXPONENT, None, ALU.bitwise_and))
            step(nc.vector.tensor_scalar(two_over_p[:, :].bitcast(I32), p_j[:, :].bitcast(I32), EXPONENT, None, ALU.bitwise_xor))
            step(nc.vector.tensor_scalar(sc[:, 7:8], sc[:, 6:7], sc[:, 3:4], None, ALU.mult))
            step(nc.vector.tensor_scalar(sc[:, 8:9].bitcast(I32), sc[:, 7:8].bitcast(I32), EXPONENT, EXPONENT,
                                         ALU.bitwise_and, ALU.bitwise_xor))
            step(nc.vector.tensor_scalar(sc[:, 8:9], sc[:, 8:9], HEADROOM, None, ALU.mult))
            for k in range(2):
                ins = nc.vector.scalar_tensor_tensor(out=c_j[:, k, :], in0=c_j[:, k, :], scalar=sc[:, 8:9],
                                                     in1=two_over_p[:, :], op0=ALU.mult, op1=ALU.mult)
            ins.then_inc(s_c, 1)

            dve.wait_ge(s_uv, 1)
            dve.wait_ge(s_wsum, 1)
            dve.wait_ge(s_srow, 16)

            def unit_masks(n, g, first_use):
                slot = g % 4
                dve.wait_ge(s_cast, 2 * n + 2)
                dve.wait_ge(s_m, n)
                src = rows16[:, g % 2].rearrange("p q j e -> p q (j e)").bitcast(I32)
                nc.vector.transpose(cols16[:, :, :].rearrange("p b i -> p (b i)").bitcast(I32)
                                    .rearrange("p (b q r) -> p q b r", b=G, q=4),
                                    src.rearrange("p q (b c) -> p q b c", b=G)).then_inc(s_tr, 1)
                if not first_use:
                    dve.wait_ge(s_mul, 2 * n - 6)
                for b in range(G):
                    ins = nc.vector.tensor_scalar(masks[:, slot, 0, b, :], neg_s[:, :], t_j[:, g * G + b:g * G + b + 1],
                                                  None, ALU.is_lt)
                dve.wait_ge(s_tr, n + 1)
                for b in range(G):
                    ins = nc.vector.tensor_scalar(cols16[:, b, :], cols16[:, b, :], 0.0, p_j[:, g * G + b:g * G + b + 1],
                                                  ALU.is_gt, ALU.mult)
                ins.then_inc(s_pos, 1)
                dve.wait_ge(s_pos, n + 1)
                nc.vector.tensor_tensor(masks[:, slot, 0], masks[:, slot, 0], cols16[:, :, :], ALU.mult).then_inc(s_m1, 1)
                dve.wait_ge(s_m1, n + 1)
                nc.vector.tensor_tensor(masks[:, slot, 1], cols16[:, :, :], masks[:, slot, 0], ALU.subtract).then_inc(s_m, 1)

            def low_parts(b, k):
                dve.wait_ge(s_hi, 2 * b + 1)
                nc.vector.scalar_tensor_tensor(out=Xp[:, b, 1, 0:F1], in0=wh_one[:, b, :], scalar=c_j[:, 0, bass.ds(b, 1)],
                                               in1=Xp[:, b, 0, 0:F1], op0=ALU.mult, op1=ALU.subtract).then_inc(s_lo, 1)
                dve.wait_ge(s_hi, 2 * b + 2)
                nc.vector.scalar_tensor_tensor(out=xt[:, k, 1, 0:F1], in0=wh_one[:, b, :], scalar=c_j[:, 1, bass.ds(b, 1)],
                                               in1=xt[:, k, 0, 0:F1], op0=ALU.mult, op1=ALU.subtract).then_inc(s_lo, 1)

            def finish(sblk):
                base = EPI * sblk
                for e in range(2):
                    dve.wait_ge(s_ev[e], 2 * sblk + 4)
                total = part[:, :, 0, :]
                nc.vector.tensor_tensor(total, part[:, :, 0, :], part[:, :, 1, :], ALU.add).then_inc(s_epi, 1)
                dve.wait_ge(s_epi, base + 1)
                nc.vector.tensor_scalar(den[:, 0, :], part[:, :, 0, F], 0.0, None, ALU.is_equal).then_inc(s_epi, 1)
                dve.wait_ge(s_epi, base + 2)
                nc.vector.scalar_tensor_tensor(out=den[:, 1, :], in0=den[:, 0, :], scalar=float(N), in1=part[:, :, 0, F],
                                               op0=ALU.mult, op1=ALU.add).then_inc(s_epi, 1)
                dve.wait_ge(s_epi, base + 3)
                nc.vector.reciprocal(den[:, 2, :], den[:, 1, :]).then_inc(s_epi, 1)
                dve.wait_ge(s_epi, base + 4)
                nc.vector.tensor_tensor(den[:, 3, :], den[:, 0, :], den[:, 2, :], ALU.mult).then_inc(s_epi, 1)
                dve.wait_ge(s_xres, 16 * sblk + 16)
                for e in range(2):
                    ins = nc.vector.scalar_tensor_tensor(out=res[:, e, :], in0=part[:, e, 0, 0:F], scalar=den[:, 2, e:e + 1],
                                                         in1=xres[:, e, :], op0=ALU.mult, op1=ALU.add)
                ins.then_inc(s_epi, 1)
                dve.wait_ge(s_epi, base + 6)
                for e in range(2):
                    ins = nc.vector.scalar_tensor_tensor(out=res[:, e, :], in0=sum_wh[:, :], scalar=den[:, 3, e:e + 1],
                                                         in1=res[:, e, :], op0=ALU.mult, op1=ALU.add)
                    ins.then_inc(s_epi if e == 0 else s_res, 1)

            def spread_neg_s(sblk):
                dve.wait_ge(s_stage, 16 * sblk + 16)
                nc.vector.tensor_copy(neg_s[:, :], neg_s_stage[:, :]).then_inc(s_ns, 1)
                dve.wait_ge(s_ns, sblk + 1)

            spread_neg_s(0)
            for g in range(NG):
                unit_masks(g, g, g < 4)
                with dve.Fori(g * G // 2, (g + 1) * G // 2) as pair:
                    for k in range(2):
                        low_parts(2 * pair + k, k)
            with dve.Fori(1, NSB) as s:
                spread_neg_s(s)
                for g in range(NG):
                    unit_masks(NG * s + g, g, False)
                    if g == 2:
                        finish(s - 1)
            finish(NSB - 1)

        @block.tensor
        def _(pe):
            pe.wait_ge(s_ident, 2)

            def transpose_h(b, k, first):
                pe.wait_ge(s_h, b + 1)
                if not first:
                    pe.wait_ge(s_hT, b - 1)
                for c in range(KF):
                    ins = nc.tensor.transpose(ps_hT[k][:, c * P:(c + 1) * P], h[:, k, c * P:(c + 1) * P], ident[:, :])
                ins.then_inc(s_ht, 1)

            def project(b, k, first):
                pe.wait_ge(s_hT, b + 1)
                if not first:
                    pe.wait_ge(s_wh, b - 1)
                for c in range(KF):
                    ins = nc.tensor.matmul(ps_wh[k][:, 0:F2], hT[:, k, c * P:(c + 1) * P], Wx[:, c, :],
                                           start=(c == 0), stop=(c == KF - 1))
                ins.then_inc(s_whp, 1)

            transpose_h(0, 0, True)
            transpose_h(1, 1, True)
            project(0, 0, True)
            transpose_h(2, 0, False)
            project(1, 1, True)
            with pe.Fori(1, NB // 2 - 1) as pair:
                for k in range(2):
                    transpose_h(2 * pair + k + 1, (k + 1) % 2, False)
                    project(2 * pair + k, k, False)
            transpose_h(NB - 1, 1, False)
            project(NB - 2, 0, False)
            project(NB - 1, 1, False)

            pe.wait_ge(s_diag, 1)
            pe.wait_ge(s_hT, NB)
            pe.wait_ge(s_wh, NB)
            for k in range(4):
                ins = nc.tensor.matmul(ps[k][0:NQ, :], quad[:, :], diag[:, 512 * k:512 * (k + 1)], start=True, stop=True)
            ins.then_inc(s_srow_ps, 1)
            dg = diag.rearrange("p (w i e) -> p w e i", w=SQ, e=2)
            for w in range(SQ):
                for e in range(2):
                    at = (2 * w + e) * NQ
                    ins = nc.tensor.matmul(acc[0][0][:, at:at + NQ], dg[:, w, e, :], quad[:, :], start=True, stop=True)
            ins.then_inc(s_scol_ps, 1)
            pe.wait_ge(s_sum, NB)
            for k in range(2):
                ins = nc.tensor.matmul(acc[0][1][:, 0:F], ones[:, :], wh_sum[:, k, :], start=(k == 0), stop=(k == 1))
            ins.then_inc(s_wsum_ps, 1)
            pe.wait_ge(s_si, 1)
            pe.wait_ge(s_wsum, 1)
            for e in range(2):
                pe.sem_inc(s_ev[e], 2)

            with pe.Fori(1, NSB + 1) as s:
                for g in range(NG):
                    pe.wait_ge(s_m, NG * s + g + 1 - NG)
                    pe.wait_ge(s_X, G * (g + 1))
                    for e in range(2):
                        if g == 0:
                            pe.wait_ge(s_ev[e], 2 * s)
                        for b in range(G):
                            for k in range(2):
                                lhsT = masks[:, g % 4, k, b, :].rearrange("p (i e) -> p e i", e=2)[:, e, :]
                                for part_ in range(2):
                                    ins = nc.tensor.matmul(acc[e][k][:, 0:F1], lhsT, Xp[:, g * G + b, 2 * k + part_, 0:F1],
                                                           start=(g == 0 and b == 0 and part_ == 0),
                                                           stop=(g == NG - 1 and b == G - 1 and part_ == 1))
                        ins.then_inc(s_mul, 1)


_INS = ["x", "adj", "L0_gnn_W_w", "L0_gnn_W_b", "L0_gnn_a"]


def kernel(**inputs):
    import numpy as np
    import concourse.bacc as bacc
    from concourse.bass_utils import run_bass_kernel_spmd

    nc = bacc.Bacc("TRN2", target_bir_lowering=False, num_devices=1)
    arrays, args = {}, []
    for name in _INS:
        arr = np.ascontiguousarray(inputs[name])
        arrays[f"in_{name}"] = arr
        args.append(nc.dram_tensor(f"in_{name}", arr.shape, mybir.dt.from_np(arr.dtype), kind="ExternalInput").ap())
    out = nc.dram_tensor("out", arrays["in_x"].shape, F32, kind="ExternalOutput").ap()
    gat_layer(nc, *args, out)
    r = run_bass_kernel_spmd(nc, [arrays], core_ids=[0])
    return r.results[0]["out"]
```

```python
import concourse.bass as bass
from concourse import mybir
from contextlib import ExitStack

F32 = mybir.dt.float32
F16 = mybir.dt.float16
BF16 = mybir.dt.bfloat16
I32 = mybir.dt.int32
ALU = mybir.AluOpType
ACT = mybir.ActivationFunctionType
AX = mybir.AxisListType
RMAX = bass.bass_isa.ReduceOp.max
RADD = bass.bass_isa.ReduceOp.add

P = 128
QP = 32
NQ = P // QP
SLOPE = 0.2
EPS = 1e-5
EXPONENT = 0x7F800000
HEADROOM = 2.0 ** 11


def gat_layer(nc, x, adj, W_w, W_b, a, out):
    N, F = x.shape
    F1 = F + 1
    F2 = F + 2
    SLOT = F2
    JQ = N // NQ
    NB = JQ // QP
    G = 8
    NG = NB // G
    R = 2 * P
    NSB = N // R
    NR = N // P
    SQ = NSB // NQ
    KF = F // P
    XG = 16
    AHEAD = 3

    x_cols = x.rearrange("(a b c) f -> a c b f", a=NQ, b=NB)
    x_rows = x.rearrange("(s e m) f -> s m e f", e=2, m=P)
    out_rows = out.rearrange("(s e m) f -> s m e f", e=2, m=P)
    adj_v = adj.rearrange("(s q r) (a g j) -> s a g r q j", q=R // QP, r=QP, a=NQ, g=NG)
    srow = nc.dram_tensor("neg_s_rows", [NQ, SQ * R], F32)
    srow_by_block = srow.ap().rearrange("a (w i) -> (a w) i", w=SQ)

    ctx = ExitStack()
    with ctx:
        def sb(name, shape, dt):
            return ctx.enter_context(nc.sbuf_tensor(name, shape, dt))

        def sem(name):
            return ctx.enter_context(nc.semaphore(name))

        X = sb("X", [P, NB, 4 * SLOT], F16)
        Xp = X[:, :, :].rearrange("p b (k f) -> p b k f", k=4)
        Xw = X[:, :, :].bitcast(F32)
        x_in = Xw[:, :, 0:F]
        wh_s_t = Xw[:, :, F2:2 * F2]
        wh = Xw[:, :, F2:F2 + F]
        wh_one = Xw[:, :, F2:F2 + F1]
        s_in = Xw[:, :, F2 + F]
        t_in = Xw[:, :, F2 + F1]

        flat_hi_0 = sb("flat_hi_0", [P, AHEAD, F2], F16)

        def flat_hi(b, first=False):
            return flat_hi_0[:, b, 0:F1] if first else Xp[:, b - AHEAD, 3, 0:F1]

        nat = sb("adj_rows", [P, 2, R // QP, G * QP], I32)
        rows16 = sb("adj_rows16", [P, 2, 4, G * QP, 2], BF16)
        cols16 = sb("adj_cols16", [P, G, R], BF16)
        side = sb("side", [P, G, R], BF16)
        masks = sb("masks", [P, 4, 2, G, R], BF16)
        neg_s = sb("neg_s", [P, R], F32)
        neg_s_stage = sb("neg_s_stage", [P, R], F32)
        part = sb("part", [P, 2, 2, F1], F32)
        xres = sb("xres", [P, 2, F], F32)
        res = sb("res", [P, 2, F], F32)
        den = sb("den", [P, 4, 2], F32)

        sum_wh = sb("sum_wh", [P, F], F32)
        t_j = sb("t_j", [P, NB], F32)
        p_j = sb("p_j", [P, NB], F32)
        c_j = sb("c_j", [P, 2, NB], F32)
        uv = sb("uv", [P, 2, NR], F32)
        ext = sb("ext", [P, 2], F32)
        top = sb("top", [P, 2], F32)
        sc = sb("sc", [P, 12], F32)

        free = masks[:, :, :, :, :].rearrange("p n k b r -> p (n k b r)").bitcast(F32)

        def carve(at, *shape):
            size = 1
            for d in shape:
                size *= d
            v = free[:, at:at + size]
            if len(shape) == 2:
                v = v.rearrange("p (a b) -> p a b", a=shape[0])
            if len(shape) == 3:
                v = v.rearrange("p (a b c) -> p a b c", a=shape[0], b=shape[1])
            return v, at + size

        w_max = 4 * 2 * G * R // 2
        a_row, at = carve(0, 2, F)
        prod, at = carve(at, F)
        h, at = carve(at, 2, F)
        hT, at = carve(at, 2, F)
        st, at = carve(at, XG, 6)
        guard, at = carve(at, 2, NR)
        mv, at = carve(at, XG, 2)
        rstd, at = carve(at, NB)
        shift, at = carve(at, NB)
        wh_sum, at = carve(at, 2, F)
        ones, at = carve(at, P)
        srow_sb, at = carve(at, SQ * R)
        diag, at = carve(at, SQ * R)
        Wx, at = carve(at, KF, F2)
        bias, at = carve(at, F2)
        ident, at = carve(at, P)
        quad, at = carve(at, NQ)
        t_c, at = carve(at, NB)
        neg_sj, at = carve(at, NB)
        two_over_p, at = carve(at, NB)
        s_i, at = carve(at, NR)
        assert at <= w_max, (at, w_max)

        acc = [[ctx.enter_context(nc.psum_tensor(f"acc{e}{k}", [P, 512], F32)) for k in range(2)]
               for e in range(2)]
        ps = [ctx.enter_context(nc.psum_tensor(f"ps{i}", [P, 512], F32)) for i in range(4)]
        ps_hT, ps_wh = ps[0:2], ps[2:4]

        s_par = sem("params_loaded")
        s_x = [sem(f"x_loaded{k}") for k in range(NB // XG)]
        s_nat = [sem(f"adj_loaded{k}") for k in range(2)]
        s_srow = sem("neg_s_rows_stored")
        s_stage = sem("neg_s_staged")
        s_xres = sem("xres_loaded")
        s_out = sem("out_stored")
        s_ident = sem("ident_step")
        s_wsq = sem("w_squares_in_partition")
        s_wsq_all = sem("w_squares_summed")
        s_wnorm = sem("w_norm_ready")
        s_var = sem("variance_ready")
        s_std = sem("std_ready")
        s_norm = sem("norm_factors_ready")
        s_diag = sem("diag_ready")
        s_srow_ps = sem("neg_s_rows_in_psum")
        s_scol_ps = sem("neg_s_columns_in_psum")
        s_wsum_ps = sem("sum_wh_in_psum")
        s_srow_sb = sem("neg_s_rows_ready")
        s_si = sem("s_i_ready")
        s_wsum = sem("sum_wh_ready")
        s_ext = sem("extremes_ready")
        s_top = sem("extremes_of_all_ready")
        s_dt = sem("t_centred")
        s_exp = sem("column_exps_ready")
        s_uvx = sem("row_exponents_ready")
        s_uv = sem("row_factors_ready")
        s_c = sem("column_factors_ready")
        s_chain = sem("vector_chain")
        s_bn = sem("bn_step")
        s_h = sem("h_ready")
        s_ht = sem("h_transposed")
        s_hT = sem("hT_ready")
        s_whp = sem("wh_in_psum")
        s_wh = sem("wh_ready")
        s_sum = sem("wh_summed")
        s_hi1 = sem("steep_hi_ready")
        s_hi2 = sem("flat_hi_ready")
        s_lo1 = sem("steep_lo_ready")
        s_X = sem("X_ready")
        s_relu = sem("adj_read")
        s_cast = sem("adj_cast")
        s_tr = sem("adj_transposed")
        s_side = sem("side_ready")
        s_m = sem("masks_ready")
        s_ns = sem("neg_s_ready")
        s_mul = sem("half_unit_multiplied")
        s_ev = [sem(f"acc{e}_evacuated") for e in range(2)]
        s_epi = sem("epilogue_step")
        s_res = sem("res_ready")

        EPI = 7

        block = ctx.enter_context(nc.Block())

        @block.sync
        def _(sp):
            for k in range(KF):
                sp.dma_start(Wx[:, k, 0:F], W_w[k * P:(k + 1) * P, :]).then_inc(s_par, 16)
            sp.dma_start(bias[:, 0:F], W_b.rearrange("(o f) -> o f", o=1).broadcast_to([P, F])).then_inc(s_par, 16)
            for k in range(2):
                sp.dma_start(a_row[:, k, :], a[k * F:(k + 1) * F, :].rearrange("f o -> o f").broadcast_to([P, F])).then_inc(s_par, 16)
            for k in range(NB // XG):
                for q in range(NQ):
                    sp.dma_start(x_in[QP * q:QP * (q + 1), k * XG:(k + 1) * XG, :],
                                 x_cols[q, :, k * XG:(k + 1) * XG, :]).then_inc(s_x[k], 16)

            def load_adj(sblk, g):
                for q in range(NQ):
                    sp.dma_start(nat[QP * q:QP * (q + 1), g % 2, :, :], adj_v[sblk, q, g]).then_inc(s_nat[g % 2], 16)

            def stage_neg_s(sblk):
                sp.dma_start(neg_s_stage[:, :], srow_by_block[bass.ds(sblk, 1), :].broadcast_to([P, R])).then_inc(s_stage, 16)

            def load_xres(sblk):
                sp.dma_start(xres[:, :, :], x_rows[sblk]).then_inc(s_xres, 16)

            def store(sblk):
                sp.dma_start(out_rows[sblk], res[:, :, :]).then_inc(s_out, 16)

            for g in range(NG):
                if g >= 2:
                    sp.wait_ge(s_relu, 2 * (g - 1))
                load_adj(0, g)
                if g == 1:
                    sp.wait_ge(s_srow_sb, 1)
                    sp.dma_start(srow.ap(), srow_sb[0:NQ, :]).then_inc(s_srow, 16)
                    sp.wait_ge(s_srow, 16)
                    stage_neg_s(0)
                if g == 6:
                    load_xres(0)
            with sp.Fori(1, NSB) as s:
                for g in range(NG):
                    sp.wait_ge(s_relu, 2 * NG * s + 2 * (g - 1))
                    load_adj(s, g)
                    if g == 0:
                        sp.wait_ge(s_ns, s)
                        stage_neg_s(s)
                    if g == 5:
                        sp.wait_ge(s_res, s)
                        store(s - 1)
                sp.wait_ge(s_out, 16 * s)
                load_xres(s)
            sp.wait_ge(s_res, NSB)
            store(NSB - 1)
            sp.wait_ge(s_out, 16 * NSB)

        @block.gpsimd
        def _(pool):
            nc.gpsimd.memset(ident[:, :], 0.0).then_inc(s_ident, 1)
            pool.wait_ge(s_ident, 1)
            nc.gpsimd.affine_select(out=ident[:, :], in_=ident[:, :], compare_op=ALU.not_equal, fill=1.0, base=0,
                                    pattern=[[-1, P]], channel_multiplier=1).then_inc(s_ident, 1)
            pool.wait_ge(s_wsq, 1)
            nc.gpsimd.partition_all_reduce(sc[:, 1:2], sc[:, 0:1], P, RADD).then_inc(s_wsq_all, 1)

            def add_wh(b, k, first):
                pool.wait_ge(s_wh, b + 1)
                if first:
                    nc.gpsimd.tensor_copy(wh_sum[:, k, :], wh[:, b, :]).then_inc(s_sum, 1)
                else:
                    pool.wait_ge(s_sum, b - 1)
                    nc.gpsimd.tensor_tensor(wh_sum[:, k, :], wh_sum[:, k, :], wh[:, b, :], ALU.add).then_inc(s_sum, 1)
            for k in range(2):
                add_wh(k, k, True)
            with pool.Fori(1, NB // 2) as pair:
                for k in range(2):
                    add_wh(2 * pair + k, k, False)
            pool.wait_ge(s_ext, 1)
            nc.gpsimd.partition_all_reduce(top[:, :], ext[:, :], P, RMAX).then_inc(s_top, 1)

            pool.wait_ge(s_c, 1)
            for b in range(NB):
                nc.gpsimd.tensor_scalar(Xp[:, b, 0, 0:F1], wh_one[:, b, :], c_j[:, 0, b:b + 1], None,
                                        ALU.mult).then_inc(s_hi1, 1)

        @block.scalar
        def _(act):
            act.wait_ge(s_par, 16 * (KF + 3))
            nc.scalar.activation(xres[:, :, :], Wx[:, :, 0:F], ACT.Square, accum_out=sc[:, 0:1]).then_inc(s_wsq, 1)
            act.wait_ge(s_wsq_all, 1)
            nc.scalar.activation(sc[:, 2:3], sc[:, 1:2], ACT.Sqrt, scale=float(F)).then_inc(s_wnorm, 1)

            def std(k):
                act.wait_ge(s_var, k + 1)
                v = rstd[:, k * XG:(k + 1) * XG]
                nc.scalar.activation(v, v, ACT.Sqrt).then_inc(s_std, 1)

            std(0)
            act.wait_ge(s_norm, 1)

            def normalise(b, k, first):
                if not first:
                    act.wait_ge(s_ht, b - 1)
                nc.scalar.activation(h[:, k, :], x_in[:, b, :], ACT.Relu, scale=rstd[:, bass.ds(b, 1)],
                                     bias=shift[:, bass.ds(b, 1)]).then_inc(s_h, 1)

            def copy_hT(b, k, first):
                act.wait_ge(s_ht, b + 1)
                if not first:
                    act.wait_ge(s_whp, b - 1)
                nc.scalar.copy(hT[:, k, :], ps_hT[k][:, 0:F]).then_inc(s_hT, 1)

            normalise(0, 0, True)
            normalise(1, 1, True)
            copy_hT(0, 0, True)
            normalise(2, 0, False)
            copy_hT(1, 1, True)

            def pairs(lo, hi):
                with act.Fori(lo, hi) as pair:
                    for k in range(2):
                        normalise(2 * pair + k + 1, (k + 1) % 2, False)
                        copy_hT(2 * pair + k, k, False)

            at_pair = 1
            for k in range(1, NB // XG):
                turn = k * XG // 2
                pairs(at_pair, turn - 2)
                std(k)
                pairs(turn - 2, turn - 1)
                act.wait_ge(s_norm, k + 1)
                at_pair = turn - 1
            pairs(at_pair, NB // 2 - 1)
            normalise(NB - 1, 1, False)
            copy_hT(NB - 2, 0, False)
            copy_hT(NB - 1, 1, False)

            def cast(n, g, first):
                act.wait_ge(s_nat[g % 2], NQ * 8 * n + NQ * 8 * (2 - g % 2))
                if not first:
                    act.wait_ge(s_tr, n - 1)
                for e in range(2):
                    nc.scalar.activation(rows16[:, g % 2, :, :, e], nat[:, g % 2, 4 * e:4 * e + 4, :],
                                         ACT.Relu).then_inc(s_relu, 1)
                act.wait_ge(s_relu, 2 * n + 2)
                flat = rows16[:, g % 2].rearrange("p q j e -> p (q j e)")
                nc.scalar.sign(flat, flat).then_inc(s_cast, 1)

            act.wait_ge(s_srow_ps, 1)
            for k in range(4):
                ins = nc.scalar.copy(srow_sb[0:NQ, 512 * k:512 * (k + 1)], ps[k][0:NQ, :])
            ins.then_inc(s_srow_sb, 1)
            act.wait_ge(s_scol_ps, 1)
            s_cols = acc[0][0][:, 0:NR].rearrange("p (w e a) -> p a w e", e=2, a=NQ)
            for q in range(NQ):
                ins = nc.scalar.mul(s_i[:, q * 2 * SQ:(q + 1) * 2 * SQ].rearrange("p (w e) -> p w e", e=2),
                                    s_cols[:, q, :, :], -1.0)
            ins.then_inc(s_si, 1)
            act.wait_ge(s_wsum_ps, 1)
            nc.scalar.copy(sum_wh[:, :], acc[0][1][:, 0:F]).then_inc(s_wsum, 1)
            act.wait_ge(s_dt, 1)
            nc.scalar.activation(c_j[:, 0, :], t_c[:, :], ACT.Exp)
            nc.scalar.activation(c_j[:, 1, :], t_c[:, :], ACT.Exp, scale=SLOPE)
            nc.scalar.activation(p_j[:, :], t_c[:, :], ACT.Exp, scale=1.0 - SLOPE)
            nc.scalar.activation(sc[:, 6:7], sc[:, 5:6], ACT.Exp, scale=SLOPE).then_inc(s_exp, 1)
            act.wait_ge(s_uvx, 1)
            nc.scalar.activation(uv[:, :, :], uv[:, :, :], ACT.Exp).then_inc(s_uv, 1)
            for g in range(2):
                cast(g, g, True)
            act.wait_ge(s_c, 1)

            def high_part(b, first):
                if not first:
                    act.wait_ge(s_X, b - AHEAD + 1)
                nc.scalar.mul(flat_hi(b, first), wh_one[:, b, :], c_j[:, 1, bass.ds(b, 1)]).then_inc(s_hi2, 1)

            def evacuate(sblk):
                for e in range(2):
                    act.wait_ge(s_mul, 2 * NG * sblk + 2 * NG - 1 + e)
                    for k in range(2):
                        nc.scalar.mul(part[:, e, k, :], acc[e][k][:, 0:F1],
                                      uv[:, k, bass.ds(2 * sblk + e, 1)]).then_inc(s_ev[e], 1)

            for g in range(NG):
                if g == 0:
                    for b in range(AHEAD + 1):
                        high_part(b, b < AHEAD)
                with act.Fori(g * G if g else AHEAD + 1, (g + 1) * G) as b:
                    high_part(b, False)
                if g + 2 < NG:
                    cast(g + 2, g + 2, False)
            with act.Fori(1, NSB) as s:
                for g in range(NG):
                    cast(NG * s + g, g, False)
                    if g == 1:
                        evacuate(s - 1)
            evacuate(NSB - 1)

        @block.vector
        def _(dve):
            steps = [0]

            def step(ins):
                steps[0] += 1
                ins.then_inc(s_chain, 1)
                dve.wait_ge(s_chain, steps[0])

            dve.wait_ge(s_par, 16 * (KF + 3))
            for k in range(KF):
                for n in range(2):
                    step(nc.vector.tensor_tensor_reduce(out=prod[:, :], in0=Wx[:, k, 0:F], in1=a_row[:, n, :],
                                                        scale=1.0, scalar=0.0, op0=ALU.mult, op1=ALU.add,
                                                        accum_out=Wx[:, k, F + n:F + n + 1]))
            for n in range(2):
                step(nc.vector.tensor_tensor_reduce(out=prod[:, :], in0=bias[:, 0:F], in1=a_row[:, n, :],
                                                    scale=1.0, scalar=0.0, op0=ALU.mult, op1=ALU.add,
                                                    accum_out=bias[:, F + n:F + n + 1]))
            step(nc.vector.memset(ones[:, :], 1.0))
            step(nc.vector.tensor_reduce(sc[:, 3:4], bias[:, 0:F], AX.X, ALU.max, apply_absolute_value=True))
            step(nc.vector.memset(quad[:, :], 0.0))
            for q in range(NQ):
                step(nc.vector.memset(quad[QP * q:QP * (q + 1), q:q + 1], 1.0))

            def stats(b, n):
                nc.vector.bn_stats(st[:, n, :], x_in[:, b, :]).then_inc(s_bn, 1)

            def norm(k):
                cols = slice(k * XG, (k + 1) * XG)
                dve.wait_ge(s_bn, (k + 1) * XG)
                for n in range(XG):
                    ins = nc.vector.bn_aggr(mv[:, n, :], st[:, n, :])
                step(ins)
                nc.vector.tensor_scalar(rstd[:, cols], mv[:, :, 1], EPS, None, ALU.add).then_inc(s_var, 1)
                dve.wait_ge(s_std, k + 1)
                step(nc.vector.reciprocal(rstd[:, cols], rstd[:, cols]))
                ins = nc.vector.scalar_tensor_tensor(out=shift[:, cols], in0=mv[:, :, 0], scalar=-1.0, in1=rstd[:, cols],
                                                     op0=ALU.mult, op1=ALU.mult)
                ins.then_inc(s_norm, 1)
                dve.wait_ge(s_norm, k + 1)

            def add_bias(b, k):
                dve.wait_ge(s_whp, b + 1)
                nc.vector.tensor_tensor(wh_s_t[:, b, :], ps_wh[k][:, 0:F2], bias[:, :], ALU.add).then_inc(s_wh, 1)

            dve.wait_ge(s_x[0], 16 * NQ)
            for n in range(XG):
                stats(n, n)
            norm(0)
            for k in range(NB // XG):
                first, half, last = k * XG // 2, (2 * k + 1) * XG // 4, (k + 1) * XG // 2
                more = k + 1 < NB // XG
                if more:
                    dve.wait_ge(s_x[k + 1], 16 * NQ)
                for pair in range(first, half):
                    for n in range(2):
                        add_bias(2 * pair + n, n)
                    if more:
                        for n in range(4 * (pair - first), 4 * (pair - first) + 4):
                            stats((k + 1) * XG + n, n)
                if more:
                    norm(k + 1)
                with dve.Fori(half, last) as pair:
                    for n in range(2):
                        add_bias(2 * pair + n, n)
            dve.wait_ge(s_wh, NB)

            step(nc.vector.tensor_scalar(neg_sj[:, :], s_in, -1.0, None, ALU.mult))
            step(nc.vector.tensor_copy(t_j[:, :], t_in))
            dve.wait_ge(s_ident, 2)
            for q in range(NQ):
                step(nc.vector.tensor_copy(prod[QP * q:QP * (q + 1), 0:QP],
                                           ident[QP * q:QP * (q + 1), QP * q:QP * (q + 1)]))
            dg = diag.rearrange("p (w q r e) -> p w q r e", w=SQ, q=4, e=2)
            ns = neg_sj[:, :].rearrange("p (w e q) -> p w q e", w=SQ, e=2)
            for w in range(SQ):
                ins = nc.vector.tensor_tensor(dg[:, w], prod[:, 0:QP].unsqueeze(1).unsqueeze(3).broadcast_to([P, 4, QP, 2]),
                                              ns[:, w].unsqueeze(2).broadcast_to([P, 4, QP, 2]), ALU.mult)
            ins.then_inc(s_diag, 1)
            nc.vector.tensor_reduce(ext[:, 0:1], t_j[:, :], AX.X, ALU.max)
            step(nc.vector.tensor_reduce(sc[:, 4:5], t_j[:, :], AX.X, ALU.min))
            nc.vector.tensor_scalar(ext[:, 1:2], sc[:, 4:5], -1.0, None, ALU.mult).then_inc(s_ext, 1)
            step(nc.vector.memset(s_in, 1.0))
            dve.wait_ge(s_wnorm, 1)
            step(nc.vector.tensor_scalar(sc[:, 3:4], sc[:, 3:4], sc[:, 2:3], 1.0, ALU.add, ALU.max))
            dve.wait_ge(s_top, 1)
            step(nc.vector.tensor_scalar(sc[:, 9:10], top[:, 1:2], -1.0, None, ALU.mult))
            step(nc.vector.tensor_scalar(sc[:, 5:6], top[:, 0:1], top[:, 1:2], None, ALU.add))
            nc.vector.tensor_scalar(t_c[:, :], t_j[:, :], sc[:, 9:10], None, ALU.subtract).then_inc(s_dt, 1)
            dve.wait_ge(s_si, 1)
            step(nc.vector.tensor_scalar(guard[:, 0, :], s_i[:, :], top[:, 0:1], None, ALU.add))
            step(nc.vector.scalar_tensor_tensor(out=guard[:, 1, :], in0=guard[:, 0, :], scalar=SLOPE, in1=guard[:, 0, :],
                                                op0=ALU.mult, op1=ALU.max))
            step(nc.vector.tensor_scalar(s_i[:, :], s_i[:, :], sc[:, 9:10], None, ALU.add))
            step(nc.vector.scalar_tensor_tensor(out=uv[:, 0, :], in0=s_i[:, :], scalar=1.0, in1=guard[:, 1, :],
                                                op0=ALU.mult, op1=ALU.subtract))
            nc.vector.scalar_tensor_tensor(out=uv[:, 1, :], in0=s_i[:, :], scalar=SLOPE, in1=guard[:, 1, :],
                                           op0=ALU.mult, op1=ALU.subtract).then_inc(s_uvx, 1)
            dve.wait_ge(s_exp, 1)
            step(nc.vector.tensor_scalar(p_j[:, :], p_j[:, :], 1.0, None, ALU.max))
            step(nc.vector.tensor_scalar(p_j[:, :].bitcast(I32), p_j[:, :].bitcast(I32), EXPONENT, None, ALU.bitwise_and))
            step(nc.vector.tensor_scalar(two_over_p[:, :].bitcast(I32), p_j[:, :].bitcast(I32), EXPONENT, None, ALU.bitwise_xor))
            step(nc.vector.tensor_scalar(sc[:, 7:8], sc[:, 6:7], sc[:, 3:4], None, ALU.mult))
            step(nc.vector.tensor_scalar(sc[:, 8:9].bitcast(I32), sc[:, 7:8].bitcast(I32), EXPONENT, EXPONENT,
                                         ALU.bitwise_and, ALU.bitwise_xor))
            step(nc.vector.tensor_scalar(sc[:, 8:9], sc[:, 8:9], HEADROOM, None, ALU.mult))
            step(nc.vector.tensor_scalar(c_j[:, 1, :], c_j[:, 1, :], sc[:, 8:9], 2.0, ALU.mult, ALU.mult))
            nc.vector.scalar_tensor_tensor(out=c_j[:, 0, :], in0=c_j[:, 0, :], scalar=sc[:, 8:9],
                                           in1=two_over_p[:, :], op0=ALU.mult, op1=ALU.mult).then_inc(s_c, 1)

            dve.wait_ge(s_uv, 1)
            dve.wait_ge(s_wsum, 1)
            dve.wait_ge(s_srow, 16)

            def unit_masks(n, g, first_use):
                slot = g % 4
                dve.wait_ge(s_cast, n + 1)
                dve.wait_ge(s_m, 2 * n)
                src = rows16[:, g % 2].rearrange("p q j e -> p q (j e)").bitcast(I32)
                nc.vector.transpose(cols16[:, :, :].rearrange("p b i -> p (b i)").bitcast(I32)
                                    .rearrange("p (b q r) -> p q b r", b=G, q=4),
                                    src.rearrange("p q (b c) -> p q b c", b=G)).then_inc(s_tr, 1)
                if not first_use:
                    dve.wait_ge(s_mul, 2 * n - 6)
                for b in range(G):
                    col = slice(g * G + b, g * G + b + 1)
                    ins = nc.vector.tensor_scalar(side[:, b, :], neg_s[:, :], t_j[:, col], p_j[:, col],
                                                  ALU.is_lt, ALU.mult)
                ins.then_inc(s_side, 1)
                dve.wait_ge(s_tr, n + 1)
                dve.wait_ge(s_side, n + 1)
                nc.vector.tensor_tensor(masks[:, slot, 0], side[:, :, :], cols16[:, :, :], ALU.mult).then_inc(s_m, 1)
                nc.vector.tensor_tensor(masks[:, slot, 1], cols16[:, :, :], side[:, :, :], ALU.is_gt).then_inc(s_m, 1)

            def steep_low(b):
                dve.wait_ge(s_hi1, b + 1)
                nc.vector.scalar_tensor_tensor(out=Xp[:, b, 1, 0:F1], in0=wh_one[:, b, :], scalar=c_j[:, 0, bass.ds(b, 1)],
                                               in1=Xp[:, b, 0, 0:F1], op0=ALU.mult, op1=ALU.subtract).then_inc(s_lo1, 1)

            def flat_low(b, first):
                dve.wait_ge(s_hi2, b + 1)
                dve.wait_ge(s_lo1, b + 1)
                nc.vector.scalar_tensor_tensor(out=Xp[:, b, 2, 0:F1], in0=wh_one[:, b, :], scalar=c_j[:, 1, bass.ds(b, 1)],
                                               in1=flat_hi(b, first), op0=ALU.mult, op1=ALU.subtract).then_inc(s_X, 1)

            def finish(sblk):
                base = EPI * sblk
                for e in range(2):
                    dve.wait_ge(s_ev[e], 2 * sblk + 4)
                total = part[:, :, 0, :]
                nc.vector.tensor_tensor(total, part[:, :, 0, :], part[:, :, 1, :], ALU.add).then_inc(s_epi, 1)
                dve.wait_ge(s_epi, base + 1)
                nc.vector.tensor_scalar(den[:, 0, :], part[:, :, 0, F], 0.0, None, ALU.is_equal).then_inc(s_epi, 1)
                dve.wait_ge(s_epi, base + 2)
                nc.vector.scalar_tensor_tensor(out=den[:, 1, :], in0=den[:, 0, :], scalar=float(N), in1=part[:, :, 0, F],
                                               op0=ALU.mult, op1=ALU.add).then_inc(s_epi, 1)
                dve.wait_ge(s_epi, base + 3)
                nc.vector.reciprocal(den[:, 2, :], den[:, 1, :]).then_inc(s_epi, 1)
                dve.wait_ge(s_epi, base + 4)
                nc.vector.tensor_tensor(den[:, 3, :], den[:, 0, :], den[:, 2, :], ALU.mult).then_inc(s_epi, 1)
                dve.wait_ge(s_xres, 16 * sblk + 16)
                for e in range(2):
                    ins = nc.vector.scalar_tensor_tensor(out=res[:, e, :], in0=part[:, e, 0, 0:F], scalar=den[:, 2, e:e + 1],
                                                         in1=xres[:, e, :], op0=ALU.mult, op1=ALU.add)
                ins.then_inc(s_epi, 1)
                dve.wait_ge(s_epi, base + 6)
                for e in range(2):
                    ins = nc.vector.scalar_tensor_tensor(out=res[:, e, :], in0=sum_wh[:, :], scalar=den[:, 3, e:e + 1],
                                                         in1=res[:, e, :], op0=ALU.mult, op1=ALU.add)
                    ins.then_inc(s_epi if e == 0 else s_res, 1)

            def spread_neg_s(sblk):
                dve.wait_ge(s_stage, 16 * sblk + 16)
                nc.vector.tensor_copy(neg_s[:, :], neg_s_stage[:, :]).then_inc(s_ns, 1)
                dve.wait_ge(s_ns, sblk + 1)

            spread_neg_s(0)
            for g in range(NG):
                unit_masks(g, g, g < 4)
                if g == 0:
                    for b in range(0, AHEAD + 1, 2):
                        for k in range(2):
                            steep_low(b + k)
                        for k in range(2):
                            flat_low(b + k, b + k < AHEAD)
                with dve.Fori(g * G // 2 if g else (AHEAD + 1) // 2, (g + 1) * G // 2) as pair:
                    for k in range(2):
                        steep_low(2 * pair + k)
                    for k in range(2):
                        flat_low(2 * pair + k, False)
            with dve.Fori(1, NSB) as s:
                spread_neg_s(s)
                for g in range(NG):
                    unit_masks(NG * s + g, g, False)
                    if g == 2:
                        finish(s - 1)
            finish(NSB - 1)

        @block.tensor
        def _(pe):
            pe.wait_ge(s_ident, 2)

            def transpose_h(b, k, first):
                pe.wait_ge(s_h, b + 1)
                if not first:
                    pe.wait_ge(s_hT, b - 1)
                for c in range(KF):
                    ins = nc.tensor.transpose(ps_hT[k][:, c * P:(c + 1) * P], h[:, k, c * P:(c + 1) * P], ident[:, :])
                ins.then_inc(s_ht, 1)

            def project(b, k, first):
                pe.wait_ge(s_hT, b + 1)
                if not first:
                    pe.wait_ge(s_wh, b - 1)
                for c in range(KF):
                    ins = nc.tensor.matmul(ps_wh[k][:, 0:F2], hT[:, k, c * P:(c + 1) * P], Wx[:, c, :],
                                           start=(c == 0), stop=(c == KF - 1))
                ins.then_inc(s_whp, 1)

            transpose_h(0, 0, True)
            transpose_h(1, 1, True)
            project(0, 0, True)
            transpose_h(2, 0, False)
            project(1, 1, True)
            with pe.Fori(1, NB // 2 - 1) as pair:
                for k in range(2):
                    transpose_h(2 * pair + k + 1, (k + 1) % 2, False)
                    project(2 * pair + k, k, False)
            transpose_h(NB - 1, 1, False)
            project(NB - 2, 0, False)
            project(NB - 1, 1, False)

            pe.wait_ge(s_diag, 1)
            pe.wait_ge(s_hT, NB)
            pe.wait_ge(s_wh, NB)
            for k in range(4):
                ins = nc.tensor.matmul(ps[k][0:NQ, :], quad[:, :], diag[:, 512 * k:512 * (k + 1)], start=True, stop=True)
            ins.then_inc(s_srow_ps, 1)
            dg = diag.rearrange("p (w i e) -> p w e i", w=SQ, e=2)
            for w in range(SQ):
                for e in range(2):
                    at = (2 * w + e) * NQ
                    ins = nc.tensor.matmul(acc[0][0][:, at:at + NQ], dg[:, w, e, :], quad[:, :], start=True, stop=True)
            ins.then_inc(s_scol_ps, 1)
            pe.wait_ge(s_sum, NB)
            for k in range(2):
                ins = nc.tensor.matmul(acc[0][1][:, 0:F], ones[:, :], wh_sum[:, k, :], start=(k == 0), stop=(k == 1))
            ins.then_inc(s_wsum_ps, 1)
            pe.wait_ge(s_si, 1)
            pe.wait_ge(s_wsum, 1)
            for e in range(2):
                pe.sem_inc(s_ev[e], 2)

            with pe.Fori(1, NSB + 1) as s:
                for g in range(NG):
                    pe.wait_ge(s_m, 2 * (NG * s + g + 1 - NG))
                    pe.wait_ge(s_X, G * (g + 1))
                    for e in range(2):
                        if g == 0:
                            pe.wait_ge(s_ev[e], 2 * s)
                        for b in range(G):
                            for k in range(2):
                                lhsT = masks[:, g % 4, k, b, :].rearrange("p (i e) -> p e i", e=2)[:, e, :]
                                c = g * G + b
                                parts = [Xp[:, c, 0, 0:F1], Xp[:, c, 1, 0:F1]] if k == 0 else \
                                    [flat_hi(c, c < AHEAD), Xp[:, c, 2, 0:F1]]
                                for n, rhs in enumerate(parts):
                                    ins = nc.tensor.matmul(acc[e][k][:, 0:F1], lhsT, rhs, start=(c == 0 and n == 0),
                                                           stop=(c == NB - 1 and n == 1))
                        ins.then_inc(s_mul, 1)


_INS = ["x", "adj", "L0_gnn_W_w", "L0_gnn_W_b", "L0_gnn_a"]


def kernel(**inputs):
    import numpy as np
    import concourse.bacc as bacc
    from concourse.bass_utils import run_bass_kernel_spmd

    nc = bacc.Bacc("TRN2", target_bir_lowering=False, num_devices=1)
    arrays, args = {}, []
    for name in _INS:
        arr = np.ascontiguousarray(inputs[name])
        arrays[f"in_{name}"] = arr
        args.append(nc.dram_tensor(f"in_{name}", arr.shape, mybir.dt.from_np(arr.dtype), kind="ExternalInput").ap())
    out = nc.dram_tensor("out", arrays["in_x"].shape, F32, kind="ExternalOutput").ap()
    gat_layer(nc, *args, out)
    r = run_bass_kernel_spmd(nc, [arrays], core_ids=[0])
    return r.results[0]["out"]
```
